# Optimizing a Trainium2 kernel written in Bass

```python
import numpy as np
import jax
import jax.numpy as jnp

def _softmax(x, axis=-1):
    return jax.nn.softmax(x, axis=axis)
def _gelu(x):
    return jax.nn.gelu(x, approximate=True)
def _silu(x):
    return jax.nn.silu(x)
def _sigmoid(x):
    return jax.nn.sigmoid(x)
def _layernorm(x, axis=-1, eps=1e-5):
    m = jnp.mean(x, axis=axis, keepdims=True)
    v = jnp.var(x, axis=axis, keepdims=True)
    return (x - m) / jnp.sqrt(v + eps)
def _scatter_add(tgt, idx, src, axis=0):
    return tgt.at[idx].add(src)
def _segment_sum(src, seg, n):
    return jax.ops.segment_sum(src, seg, n)

kernel_name = 'mk_adj_preln_d1_adj_1024_ce7db2'

def setup_inputs(seed: int = 0):
    np.random.seed(seed)
    _w = jnp.asarray
    def _rec_inputs():
        import jax
        import jax.numpy as jnp
        _gk = jax.random.key(seed)
        x = -0.0003929 + 0.9999 * jax.random.normal(jax.random.fold_in(_gk, 1), (32, 512, 1024), jnp.float32)
        _w = (1.0 + jnp.arange(512, dtype=jnp.float32)) ** -0.5
        _w = _w / _w.mean()
        _pij = jnp.clip(0.0078125 * _w[:, None] * _w[None, :], 0.0, 1.0)
        _a = jax.random.uniform(jax.random.fold_in(_gk, 2), (512, 512)) < _pij
        _a = jnp.logical_or(_a, jnp.swapaxes(_a, -1, -2))
        _a = jnp.logical_or(_a, jnp.eye(512, dtype=bool))
        _af = _a.astype(jnp.float32)
        _af = _af * jax.random.uniform(jax.random.fold_in(_gk, 3), (512, 512), jnp.float32, 0.05, 0.198159)
        adj = _af
        return x, adj
    x, adj = _rec_inputs()
    def _L0_gnn_setup():
        import jax, jax.numpy as jnp
        import numpy as np
        NEG_SLOPE = 0.01
        key = jax.random.key(seed)
        k1, k2, k3, k4, k5 = jax.random.split(key, 5)
        B, C, N, O = (32, 512, 1024, 512)
        x = jax.random.normal(k1, (B, C, N), dtype=jnp.float32)
        wq = jax.random.normal(k2, (C,), dtype=jnp.float32) * (1.0 / np.sqrt(C))
        wk = jax.random.normal(k3, (C,), dtype=jnp.float32) * (1.0 / np.sqrt(C))
        wm = jax.random.normal(k4, (O, C), dtype=jnp.float32) * (1.0 / np.sqrt(C))
        bm = jax.random.normal(k5, (O,), dtype=jnp.float32) * 0.01
        return {'x': x, 'wq': wq, 'wk': wk, 'wm': wm, 'bm': bm}
    _L0_gnn_all = _L0_gnn_setup()
    _L0_gnn_in = {k: v for k, v in _L0_gnn_all.items() if k in ('wq', 'wk', 'bm', )}
    del _L0_gnn_all

    return {
        "x": x,
        "adj": adj,
        "L0_gnn_wq": _L0_gnn_in["wq"],
        "L0_gnn_wk": _L0_gnn_in["wk"],
        "L0_gnn_bm": _L0_gnn_in["bm"],
    }

def reference(x, adj, L0_gnn_wq, L0_gnn_wk, L0_gnn_bm):
    import jax
    import jax.numpy as jnp
    def _L0_gnn_ref(x, wq, wk, wm, bm):
        import jax, jax.numpy as jnp
        import numpy as np
        NEG_SLOPE = 0.01
        q = jnp.einsum('c,bcn->bn', wq, x)
        k = jnp.einsum('c,bcn->bn', wk, x)
        scores = q[:, None, :] + k[:, :, None]
        scores = jnp.where(scores > 0, scores, NEG_SLOPE * scores)
        att = jax.nn.softmax(scores, axis=-1)
        agg = jnp.einsum('bcn,bmn->bcm', x, att)
        out = jnp.einsum('oc,bcm->bom', wm, agg) + bm[None, :, None]
        return jax.nn.relu(out)

    h = jnp.maximum(_layernorm(x, axis=-1), 0.0)
    x = x + _L0_gnn_ref(h, L0_gnn_wq, L0_gnn_wk, adj, L0_gnn_bm)
    return x


_drawn_inputs = setup_inputs


def setup_inputs(seed=0):
    import zlib

    import numpy as np

    out = dict(_drawn_inputs(seed))
    spreads = {}
    factors = {'L0_gnn_wq': 8.0, 'L0_gnn_wk': 8.0, 'L0_gnn_bm': 6.631}
    for name, (base, spread) in spreads.items():
        noise = np.random.default_rng([zlib.crc32(name.encode()), seed]).standard_normal(out[name].shape)
        drawn = base * np.exp(spread * noise) if base else spread * noise
        out[name] = jnp.asarray(drawn.astype(out[name].dtype))
    for name, factor in factors.items():
        out[name] = (out[name] * factor).astype(out[name].dtype)
    return out
```

```python
from contextlib import ExitStack

import concourse.bass as bass
from concourse import mybir

F32 = mybir.dt.float32
F16 = mybir.dt.float16
I32 = mybir.dt.int32
ALU = mybir.AluOpType
ACT = mybir.ActivationFunctionType
AX = mybir.AxisListType

P = 128
H_SCALE = 2.0 ** 10
P_SCALE = 2.0 ** 15
V_BITS = 2.0 ** 9
Q_BITS = 2.0 ** 12
EPS = 1e-5
LEAK = 0.01
NEWTON = 3


def gnn_layer(nc, x, adj, wq, wk, bm, out):
    B, C, N = x.shape
    O = adj.shape[0]
    CT, NT, OT = C // P, N // P, O // P
    HALF = N // 2
    MT = HALF // P
    U = 2 * OT
    G = 2 * NT
    assert C == O == 512 and HALF == 512 and B % 2 == 0
    PAIRS = B // 2 - 1

    with ExitStack() as ctx:
        def sb(name, shape, dt=F32):
            return ctx.enter_context(nc.sbuf_tensor(name, shape, dt))

        def bank(name):
            return ctx.enter_context(nc.psum_tensor(name, [P, 512], F32))

        def sem(name):
            return ctx.enter_context(nc.semaphore(name))

        xs = sb("xs", [P, 2, CT, N])
        h_hi = sb("h_hi", [P, 2, CT, N], F16)
        h_lo = sb("h_lo", [P, 2, CT, N], F16)
        h32 = sb("h32", [P, 2, N])
        v_hi = sb("v_hi", [P, NT, O], F16)
        v_lo = sb("v_lo", [P, NT, O], F16)
        p_hi = sb("p_hi", [P, 2, NT, HALF], F16)
        p_lo = sb("p_lo", [P, 2, NT, HALF], F16)
        p32 = sb("p32", [P, 4, HALF])
        leak32 = sb("leak32", [P, 4, HALF])
        psum_n = sb("psum_n", [P, 2, HALF])
        rden = sb("rden", [P, 2, HALF])
        z = sb("z", [P, 2, HALF])
        res = sb("res", [P, U, HALF])
        wmT_hi = sb("wmT_hi", [P, CT, O], F16)
        wmT_lo = sb("wmT_lo", [P, CT, O], F16)
        wqk = sb("wqk", [P, CT, 4], F16)
        ident = sb("ident", [P, P])
        ones = sb("ones", [P, 1])
        bias_o = sb("bias_o", [P, OT])
        unscale_o = sb("unscale_o", [P, OT])
        unscale_q = sb("unscale_q", [P, 2])
        wm_nat = xs[:, 1, :, 0:C]
        wqk_row = res[:, 0:2, :]
        scrap = res[:, 2:8, :]
        wqk_col = sb("wqk_col", [P, 2, CT])
        rows = sb("rows", [P, OT + 2])
        pow2 = sb("pow2", [P, OT + 2])
        inv2 = sb("inv2", [P, OT + 2])
        stats = sb("stats", [P, CT, 2, 6])
        moments = sb("moments", [P, CT, 2])
        var_eps = sb("var_eps", [P, CT])
        rstd = sb("rstd", [P, CT])
        half_y2 = sb("half_y2", [P, CT])
        t_y = sb("t_y", [P, CT])
        ln_scale = sb("ln_scale", [P, 2, CT])
        ln_shift = sb("ln_shift", [P, 2, CT])
        qk4 = sb("qk4", [P, NT, 4])
        qk = sb("qk", [P, 2, NT])
        qs = sb("qs", [P, 2, NT])
        qmax_p = sb("qmax_p", [P, 1])
        qmax = sb("qmax", [P, 1])
        zcol = sb("zcol", [P, NT])
        earg = sb("earg", [P, 4, NT])
        ecol = sb("ecol", [P, 4, NT])
        AB = sb("AB", [P, 2, NT])
        rcol = sb("rcol", [P, 2, MT])

        acc = [bank("acc0"), bank("acc1")]
        vps = [bank("vps0"), bank("vps1")]
        a_ps, b_ps, r_ps = bank("a_ps"), bank("b_ps"), bank("r_ps")
        small = bank("small")
        qk_ps = small[:, 0:4 * NT].rearrange("p (t j) -> p t j", j=4)
        den_ps = small[:, 64:64 + 2 * MT].rearrange("p (h t) -> p h t", h=2)
        qmax_ps = small[:, 128:256]

        s_w = sem("weights_loaded")
        s_wx = sem("x1_may_load")
        s_x = [[sem(f"x_loaded_{j}_{c}") for c in range(CT)] for j in range(2)]
        s_id = sem("constants_ready")
        s_abs = sem("abs_sums")
        s_su = sem("setup_vector")
        s_wt = sem("wmT_transposed")
        s_wh = sem("wmT_hi_ready")
        s_wl = sem("wmT_lo_ready")
        s_ln = sem("ln_chain")
        s_h32 = sem("h32_ready")
        s_hlo = sem("h_split")
        s_qk = sem("qk_done")
        s_qc = sem("q_chain")
        s_qmT = sem("qmax_spread")
        s_exp = sem("exponentials")
        s_bc = sem("ab_spread")
        s_lk = sem("leak_ready")
        s_p = sem("numerator_ready")
        s_phi = sem("p_hi_ready")
        s_plo = sem("p_lo_ready")
        s_sum = sem("numerator_summed")
        s_den = sem("denominator")
        s_rc = sem("reciprocal")
        s_rT = sem("reciprocal_spread")
        s_rd = sem("rden_ready")
        s_v = sem("v_psum_done")
        s_vhi = sem("v_hi_ready")
        s_vlo = [sem(f"v_split_{i}") for i in range(2)]
        s_acc = sem("unit_accumulated")
        s_z = [sem(f"z_ready_{i}") for i in range(2)]
        s_y = [sem(f"relu_done_{i}") for i in range(2)]
        s_add = sem("unit_finished")
        s_st = [sem(f"stored_{k}") for k in range(U)]

        def nxt(b, by=1):
            j = b[1] + by
            return (b[0] + j // 2, j % 2)

        def cnt(b, per, n):
            return b[0] * (2 * per) + (b[1] * per + n)

        def wait(eng, semaphore, value):
            if not (isinstance(value, int) and value <= 0):
                eng.wait_ge(semaphore, value)

        first = (0, 0)

        LN_OPS = 3 + 3 * NEWTON + 2 + 1
        Q_OPS = 12

        block = ctx.enter_context(nc.Block())

        @block.sync
        def _(sp):
            def load_x(b, c):
                src = x[b[0] * 2 + b[1], c * P:(c + 1) * P, :]
                sp.dma_start(xs[:, b[1], c, :], src).then_inc(s_x[b[1]][c], 16)

            def store(b, k):
                hf, ot = divmod(k, OT)
                sp.wait_ge(s_add, cnt(b, U, k + 1))
                dst = out[b[0] * 2 + b[1], ot * P:(ot + 1) * P, hf * HALF:(hf + 1) * HALF]
                sp.dma_start(dst, res[:, k, :]).then_inc(s_st[k], 16)

            for c in range(CT):
                load_x(first, c)
            sp.dma_start(wm_nat, adj.rearrange("(t p) c -> p t c", p=P)).then_inc(s_w, 16)
            for i, w in enumerate((wq, wk)):
                sp.dma_start(wqk_row[:, i, :], w.partition_broadcast(P)).then_inc(s_w, 16)
                with nc.allow_non_contiguous_dma(reason="512 weights, once"):
                    sp.dma_start(wqk_col[:, i, :], w.rearrange("(t p) -> p t", p=P)).then_inc(s_w, 16)
            with nc.allow_non_contiguous_dma(reason="512 biases, once"):
                sp.dma_start(bias_o[:, :], bm.rearrange("(t p) -> p t", p=P)).then_inc(s_w, 16)
            sp.wait_ge(s_wx, 1)
            for c in range(CT):
                load_x((0, 1), c)

            def period(b, load):
                for k in range(U):
                    store(b, k)
                    if load and k >= OT:
                        load_x(nxt(b, 2), k - OT)

            period((0, 0), True)
            period((0, 1), True)
            with sp.Fori(1, PAIRS) as i:
                period((i, 0), True)
                period((i, 1), True)
            period((PAIRS, 0), False)
            period((PAIRS, 1), False)
            for k in range(U):
                sp.wait_ge(s_st[k], 16 * B)

        @block.tensor
        def _(pe):
            def transposed_weights():
                pe.wait_ge(s_id, 3)
                pe.wait_ge(s_su, 7)
                for ct in range(CT):
                    if ct >= 2:
                        pe.wait_ge(s_wl, ct)
                    for ot in range(OT):
                        mm = pe.transpose(vps[ct % 2][:, ot * P:(ot + 1) * P],
                                          wm_nat[:, ot, ct * P:(ct + 1) * P], ident[:, :])
                    mm.then_inc(s_wt, 1)
                pe.wait_ge(s_wl, CT + 1)

            def project_qk(b):
                pe.wait_ge(s_hlo, cnt(b, CT, CT))
                for nt in range(NT):
                    for ct in range(CT):
                        for part, hp in enumerate((h_hi, h_lo)):
                            mm = pe.matmul(qk_ps[:, nt, :], hp[:, b[1], ct, nt * P:(nt + 1) * P], wqk[:, ct, :],
                                           start=(ct == 0 and part == 0), stop=(ct == CT - 1 and part == 1))
                mm.then_inc(s_qk, 1)

            def spread_qmax(b):
                pe.wait_ge(s_qc, cnt(b, Q_OPS, 5))
                pe.transpose(qmax_ps, qmax_p[:, 0:1].to_broadcast([P, P]), ident[:, :]).then_inc(s_qmT, 1)

            def spread_ab(b, hf):
                pe.wait_ge(s_exp, cnt(b, 1, 1))
                wait(pe, s_p, cnt(b, G, NT * hf))
                for which, dst in ((2, a_ps), (3, b_ps)):
                    for t in range(MT):
                        mt = hf * MT + t
                        mm = pe.transpose(dst[:, t * P:(t + 1) * P],
                                          ecol[:, which, mt:mt + 1].to_broadcast([P, P]), ident[:, :])
                mm.then_inc(s_bc, 1)

            def v_tile(b, nt):
                wait(pe, s_vlo[nt % 2], cnt(b, NT // 2, nt // 2))
                ps, cols = vps[nt % 2], slice(nt * P, (nt + 1) * P)
                for ct in range(CT):
                    hi, lo = h_hi[:, b[1], ct, cols], h_lo[:, b[1], ct, cols]
                    pe.matmul(ps[:, :], hi, wmT_hi[:, ct, :], start=(ct == 0), stop=False)
                    pe.matmul(ps[:, :], hi, wmT_lo[:, ct, :], start=False, stop=False)
                    mm = pe.matmul(ps[:, :], lo, wmT_hi[:, ct, :], start=False, stop=(ct == CT - 1))
                mm.then_inc(s_v, 1)

            def unit(b, k):
                hf, ot = divmod(k, OT)
                if ot == 0:
                    pe.wait_ge(s_plo, cnt(b, G, NT * (hf + 1)))
                wait(pe, s_z[k % 2], cnt(b, U // 2, k // 2))
                ps, cols = acc[k % 2], slice(ot * P, (ot + 1) * P)
                for nt in range(NT):
                    if k == 0:
                        pe.wait_ge(s_vlo[nt % 2], cnt(b, NT // 2, nt // 2 + 1))
                    pe.matmul(ps[:, :], v_hi[:, nt, cols], p_hi[:, hf, nt, :], start=(nt == 0), stop=False)
                    pe.matmul(ps[:, :], v_hi[:, nt, cols], p_lo[:, hf, nt, :], start=False, stop=False)
                    mm = pe.matmul(ps[:, :], v_lo[:, nt, cols], p_hi[:, hf, nt, :],
                                   start=False, stop=(nt == NT - 1))
                mm.then_inc(s_acc, 1)

            def denominator(b, hf):
                pe.wait_ge(s_sum, cnt(b, G - 2, (NT - 1) * (hf + 1)))
                for t in range(MT):
                    mm = pe.matmul(den_ps[:, hf, t:t + 1], psum_n[:, hf, t * P:(t + 1) * P], ones[:, :],
                                   start=True, stop=True)
                mm.then_inc(s_den, 1)

            def spread_reciprocal(b, hf):
                pe.wait_ge(s_rc, cnt(b, 2, hf + 1))
                for t in range(MT):
                    mm = pe.transpose(r_ps[:, t * P:(t + 1) * P],
                                      rcol[:, hf, t:t + 1].to_broadcast([P, P]), ident[:, :])
                mm.then_inc(s_rT, 1)

            def v_tiles(b):
                for nt in range(NT - 2):
                    v_tile(b, nt)
                spread_ab(b, 1)
                for nt in range(NT - 2, NT):
                    v_tile(b, nt)

            def period(b, more):
                denominator(b, 0)
                unit(b, 0)
                spread_reciprocal(b, 0)
                for k in range(1, OT):
                    unit(b, k)
                denominator(b, 1)
                unit(b, OT)
                spread_reciprocal(b, 1)
                if more:
                    project_qk(nxt(b))
                unit(b, OT + 1)
                if more:
                    spread_qmax(nxt(b))
                unit(b, OT + 2)
                if more:
                    spread_ab(nxt(b), 0)
                unit(b, OT + 3)
                if more:
                    v_tiles(nxt(b))

            transposed_weights()
            project_qk(first)
            spread_qmax(first)
            spread_ab(first, 0)
            v_tiles(first)
            period((0, 0), True)
            period((0, 1), True)
            with pe.Fori(1, PAIRS) as i:
                period((i, 0), True)
                period((i, 1), True)
            period((PAIRS, 0), True)
            period((PAIRS, 1), False)

        @block.scalar
        def _(act):
            def setup():
                act.wait_ge(s_w, 16 * 6)
                for ot in range(OT):
                    act.activation(scrap[:, ot, :], wm_nat[:, ot, :], ACT.Abs, accum_out=rows[:, ot:ot + 1]).then_inc(s_abs, 1)
                for i in range(2):
                    act.activation(scrap[:, OT + i, :], wqk_row[:, i, :], ACT.Abs,
                                   accum_out=rows[:, OT + i:OT + i + 1]).then_inc(s_abs, 1)
                for ct in range(CT):
                    act.wait_ge(s_wt, ct + 1)
                    act.activation(wmT_hi[:, ct, :], vps[ct % 2][:, :], ACT.Copy).then_inc(s_wh, 1)

            def normalise(b, ct):
                if ct == 0:
                    act.wait_ge(s_ln, cnt(b, LN_OPS, LN_OPS))
                    wait(act, s_v, cnt(b, NT, -NT))
                wait(act, s_hlo, cnt(b, CT, ct - 1))
                sc, sh = ln_scale[:, b[1], ct:ct + 1], ln_shift[:, b[1], ct:ct + 1]
                act.activation(h_hi[:, b[1], ct, :], xs[:, b[1], ct, :], ACT.Relu, bias=sh, scale=sc)
                act.activation(h32[:, ct % 2, :], xs[:, b[1], ct, :], ACT.Relu, bias=sh,
                               scale=sc).then_inc(s_h32, 1)

            def exponentials(b):
                act.wait_ge(s_qc, cnt(b, Q_OPS, 11))
                act.activation(ecol[:, :, :], earg[:, :, :], ACT.Exp).then_inc(s_exp, 1)

            def leak(b, t):
                hf, nt = divmod(t, NT)
                if nt == 0:
                    act.wait_ge(s_bc, cnt(b, 2, hf + 1))
                    act.wait_ge(s_qc, cnt(b, Q_OPS, 12))
                wait(act, s_p, cnt(b, G, t - 3))
                act.activation(leak32[:, t % 4, :], b_ps[:, :], ACT.Copy,
                               scale=AB[:, 1, nt:nt + 1]).then_inc(s_lk, 1)

            def p_upper(b, t):
                hf, nt = divmod(t, NT)
                act.wait_ge(s_p, cnt(b, G, t + 1))
                if nt == 0:
                    wait(act, s_acc, cnt(b, U, OT * (hf + 1) - U))
                act.activation(p_hi[:, hf, nt, :], p32[:, t % 4, :], ACT.Copy).then_inc(s_phi, 1)

            def v_upper(b, nt):
                act.wait_ge(s_v, cnt(b, NT, nt + 1))
                act.activation(v_hi[:, nt, :], vps[nt % 2][:, :], ACT.Copy,
                               scale=1.0 / H_SCALE).then_inc(s_vhi, 1)

            def relu(b, k):
                hf, ot = divmod(k, OT)
                act.wait_ge(s_z[k % 2], cnt(b, U // 2, k // 2 + 1))
                wait(act, s_st[k], cnt(b, 16, 0))
                act.activation(res[:, k, :], z[:, k % 2, :], ACT.Relu, bias=bias_o[:, ot:ot + 1],
                               scale=unscale_o[:, ot:ot + 1]).then_inc(s_y[k % 2], 1)

            def copy_reciprocal(b, hf):
                act.wait_ge(s_rT, cnt(b, 2, hf + 1))
                act.activation(rden[:, hf, :], r_ps[:, :], ACT.Copy).then_inc(s_rd, 1)

            def numerator_pair(b, t, between=()):
                leak(b, t)
                leak(b, t + 1)
                for f in between:
                    f()
                p_upper(b, t)
                p_upper(b, t + 1)

            def v_slots(b, before):
                for m in range(NT // 2):
                    if m == 0:
                        before()
                    v_upper(b, 2 * m)
                    numerator_pair(b, 2 * m + 2, [lambda m=m: v_upper(b, 2 * m + 1)])

            def period(b, more):
                numerator_pair(b, NT + 2)
                copy_reciprocal(b, 0)
                relu(b, 0)
                numerator_pair(b, NT + 4)
                relu(b, 1)
                numerator_pair(b, NT + 6)
                if more:
                    normalise(nxt(b), 0)
                    normalise(nxt(b), 1)
                relu(b, 2)
                if more:
                    normalise(nxt(b), 2)
                    normalise(nxt(b), 3)
                relu(b, 3)
                copy_reciprocal(b, 1)
                relu(b, 4)
                if more:
                    exponentials(nxt(b))
                relu(b, 5)
                if more:
                    numerator_pair(nxt(b), 0)
                relu(b, 6)
                if more:
                    v_slots(nxt(b), lambda: relu(b, 7))
                else:
                    relu(b, 7)

            setup()
            for ct in range(CT):
                normalise(first, ct)
            exponentials(first)
            numerator_pair(first, 0)
            v_slots(first, lambda: None)
            period((0, 0), True)
            period((0, 1), True)
            with act.Fori(1, PAIRS) as i:
                period((i, 0), True)
                period((i, 1), True)
            period((PAIRS, 0), True)
            period((PAIRS, 1), False)

        @block.vector
        def _(dve):
            def setup():
                n = [0]

                def link(ins):
                    n[0] += 1
                    ins.then_inc(s_su, 1)
                    dve.wait_ge(s_su, n[0])

                dve.memset(ones[:, :], 1.0).then_inc(s_id, 1)
                dve.wait_ge(s_abs, OT + 2)
                link(dve.tensor_scalar(rows[:, :], rows[:, :], 1e-25, 1e30, ALU.max, ALU.min))
                link(dve.tensor_scalar(pow2[:, :].bitcast(I32), rows[:, :].bitcast(I32), 0x7F800000, None,
                                       ALU.bitwise_and))
                link(dve.reciprocal(inv2[:, :], pow2[:, :]))
                for ot in range(OT):
                    ins = dve.tensor_scalar(wm_nat[:, ot, :], wm_nat[:, ot, :], inv2[:, ot:ot + 1], V_BITS,
                                            ALU.mult, ALU.mult)
                    ins.then_inc(s_su, 1)
                n[0] += OT
                for i in range(2):
                    ins = dve.tensor_scalar(wqk_col[:, i, :], wqk_col[:, i, :], inv2[:, OT + i:OT + i + 1], Q_BITS,
                                            ALU.mult, ALU.mult)
                    ins.then_inc(s_su, 1)
                dve.tensor_scalar(unscale_o[:, :], pow2[:, 0:OT], 1.0 / V_BITS, None, ALU.mult).then_inc(s_su, 1)
                dve.tensor_scalar(unscale_q[:, :], pow2[:, OT:OT + 2], 1.0 / (Q_BITS * H_SCALE), None,
                                  ALU.mult).then_inc(s_su, 1)
                n[0] += 4
                dve.wait_ge(s_su, n[0])
                hi = wqk[:, :, :].rearrange("p t (i s) -> p s i t", s=2)
                link(dve.tensor_copy(hi[:, 0], wqk_col[:, :, :]))
                dve.tensor_tensor(hi[:, 1], wqk_col[:, :, :], hi[:, 0], ALU.subtract).then_inc(s_wl, 1)
                for ct in range(CT):
                    dve.wait_ge(s_wh, ct + 1)
                    dve.tensor_tensor(wmT_lo[:, ct, :], vps[ct % 2][:, :], wmT_hi[:, ct, :],
                                      ALU.subtract).then_inc(s_wl, 1)
                dve.wait_ge(s_wt, CT)
                dve.memset(t_y[:, 0:1], 0.0).then_inc(s_wx, 1)

            def statistics(b, cts):
                for ct in cts:
                    dve.wait_ge(s_x[b[1]][ct], (b[0] + 1) * 16)
                    for s in range(2):
                        ins = dve.bn_stats(stats[:, ct, s, :], xs[:, b[1], ct, s * HALF:(s + 1) * HALF])
                if cts[-1] == CT - 1:
                    ins.then_inc(s_ln, 1)

            def normaliser(b):
                n = [1]

                def link(ins):
                    ins.then_inc(s_ln, 1)
                    n[0] += 1
                    dve.wait_ge(s_ln, cnt(b, LN_OPS, n[0]))

                dve.wait_ge(s_ln, cnt(b, LN_OPS, 1))
                dve.memset(half_y2[:, :], 0.0)
                for ct in range(CT):
                    ins = dve.bn_aggr(moments[:, ct, :], stats[:, ct, :, :].rearrange("p s j -> p (s j)"))
                link(ins)
                link(dve.tensor_scalar(var_eps[:, :], moments[:, :, 1], EPS, None, ALU.add))
                link(dve.tensor_scalar(rstd[:, :].bitcast(I32), var_eps[:, :].bitcast(I32), -0.5, float(0x5F3759DF),
                                       ALU.mult, ALU.add))
                for _ in range(NEWTON):
                    link(dve.scalar_tensor_tensor(out=half_y2[:, :], in0=rstd[:, :], scalar=-0.5, in1=rstd[:, :],
                                                  op0=ALU.mult, op1=ALU.mult))
                    link(dve.tensor_tensor(t_y[:, :], half_y2[:, :], var_eps[:, :], ALU.mult))
                    link(dve.scalar_tensor_tensor(out=rstd[:, :], in0=t_y[:, :], scalar=1.5, in1=rstd[:, :],
                                                  op0=ALU.add, op1=ALU.mult))
                link(dve.tensor_scalar(ln_scale[:, b[1], :], rstd[:, :], H_SCALE, None, ALU.mult))
                dve.scalar_tensor_tensor(out=ln_shift[:, b[1], :], in0=moments[:, :, 0], scalar=-H_SCALE,
                                         in1=rstd[:, :], op0=ALU.mult, op1=ALU.mult).then_inc(s_ln, 1)
                assert n[0] + 1 == LN_OPS

            def h_lower(b, ct):
                dve.wait_ge(s_h32, cnt(b, CT, ct + 1))
                dve.tensor_tensor(h_lo[:, b[1], ct, :], h32[:, ct % 2, :], h_hi[:, b[1], ct, :],
                                  ALU.subtract).then_inc(s_hlo, 1)

            def q_link(b, n, ins):
                ins.then_inc(s_qc, 1)
                dve.wait_ge(s_qc, cnt(b, Q_OPS, n))

            def q_head(b):
                dve.wait_ge(s_qk, cnt(b, 1, 1))
                q_link(b, 1, dve.tensor_copy(qk4[:, :, :], qk_ps))
                parts = qk4[:, :, :].rearrange("p t (i s) -> p s i t", s=2)
                q_link(b, 2, dve.tensor_tensor(qs[:, :, :], parts[:, 0], parts[:, 1], ALU.add))
                for i in range(2):
                    q_link(b, 3 + i, dve.tensor_scalar(qk[:, i, :], qs[:, i, :], unscale_q[:, i:i + 1], None,
                                                       ALU.mult))
                dve.tensor_reduce(qmax_p[:, :], qk[:, 0, :], AX.X, ALU.max).then_inc(s_qc, 1)

            def q_tail(b):
                dve.wait_ge(s_qmT, cnt(b, 1, 1))
                q_link(b, 6, dve.tensor_reduce(qmax[:, :], qmax_ps, AX.X, ALU.max))
                dve.tensor_scalar(earg[:, 0, :], qk[:, 0, :], qmax[:, 0:1], None, ALU.subtract).then_inc(s_qc, 1)
                dve.tensor_scalar(zcol[:, :], qk[:, 1, :], qmax[:, 0:1], None, ALU.add).then_inc(s_qc, 1)
                dve.wait_ge(s_qc, cnt(b, Q_OPS, 8))
                dve.tensor_scalar(earg[:, 1, :], earg[:, 0, :], LEAK, None, ALU.mult).then_inc(s_qc, 1)
                dve.tensor_scalar(earg[:, 2, :], zcol[:, :], 1.0 - LEAK, 0.0, ALU.mult, ALU.min).then_inc(s_qc, 1)
                dve.tensor_scalar(earg[:, 3, :], zcol[:, :], LEAK - 1.0, 0.0, ALU.mult, ALU.min).then_inc(s_qc, 1)
                dve.wait_ge(s_exp, cnt(b, 1, 1))
                q_link(b, 12, dve.tensor_scalar(AB[:, :, :], ecol[:, 0:2, :], P_SCALE, None, ALU.mult))

            def numerator(b, t):
                hf, nt = divmod(t, NT)
                dve.wait_ge(s_lk, cnt(b, G, t + 1))
                ago = t - 4
                wait(dve, s_sum, cnt(b, G - 2, (NT - 1) * (ago // NT) + max(ago % NT, 1)))
                dve.scalar_tensor_tensor(out=p32[:, t % 4, :], in0=a_ps[:, :], scalar=AB[:, 0, nt:nt + 1],
                                         in1=leak32[:, t % 4, :], op0=ALU.mult, op1=ALU.max).then_inc(s_p, 1)

            def p_lower(b, t):
                hf, nt = divmod(t, NT)
                dve.wait_ge(s_phi, cnt(b, G, t + 1))
                dve.tensor_tensor(p_lo[:, hf, nt, :], p32[:, t % 4, :], p_hi[:, hf, nt, :],
                                  ALU.subtract).then_inc(s_plo, 1)

            def numerator_pair(b, t, between=()):
                numerator(b, t)
                numerator(b, t + 1)
                for f in between:
                    f()
                p_lower(b, t)
                p_lower(b, t + 1)

            def v_lower(b, nt):
                dve.wait_ge(s_vhi, cnt(b, NT, nt + 1))
                dve.scalar_tensor_tensor(out=v_lo[:, nt, :], in0=vps[nt % 2][:, :], scalar=1.0 / H_SCALE,
                                         in1=v_hi[:, nt, :], op0=ALU.mult,
                                         op1=ALU.subtract).then_inc(s_vlo[nt % 2], 1)

            def reciprocal(b, hf):
                dve.wait_ge(s_den, cnt(b, 2, hf + 1))
                dve.reciprocal(rcol[:, hf, :], den_ps[:, hf, :]).then_inc(s_rc, 1)

            def normalised(b, k):
                hf, ot = divmod(k, OT)
                if ot == 0:
                    dve.wait_ge(s_rd, cnt(b, 2, hf + 1))
                dve.wait_ge(s_acc, cnt(b, U, k + 1))
                wait(dve, s_y[k % 2], cnt(b, U // 2, k // 2))
                dve.tensor_tensor(z[:, k % 2, :], acc[k % 2][:, :], rden[:, hf, :],
                                  ALU.mult).then_inc(s_z[k % 2], 1)

            def v_slots(b, before):
                for m in range(NT // 2):
                    if m == 0:
                        before()
                    v_lower(b, 2 * m)
                    numerator_pair(b, 2 * m + 2, [lambda m=m: v_lower(b, 2 * m + 1)])

            def period(b, more):
                reciprocal(b, 0)
                numerator_pair(b, NT + 2)
                if more:
                    statistics(nxt(b), [0, 1])
                normalised(b, 0)
                numerator_pair(b, NT + 4)
                if more:
                    statistics(nxt(b), [2, 3])
                    normaliser(nxt(b))
                normalised(b, 1)
                numerator_pair(b, NT + 6)
                if more:
                    h_lower(nxt(b), 0)
                normalised(b, 2)
                if more:
                    h_lower(nxt(b), 1)
                    h_lower(nxt(b), 2)
                reciprocal(b, 1)
                normalised(b, 3)
                if more:
                    h_lower(nxt(b), 3)
                normalised(b, 4)
                if more:
                    q_head(nxt(b))
                normalised(b, 5)
                if more:
                    q_tail(nxt(b))
                normalised(b, 6)
                if more:
                    numerator_pair(nxt(b), 0)
                    v_slots(nxt(b), lambda: normalised(b, 7))
                else:
                    normalised(b, 7)

            setup()
            statistics(first, [0, 1, 2, 3])
            normaliser(first)
            for ct in range(CT):
                h_lower(first, ct)
            q_head(first)
            q_tail(first)
            numerator_pair(first, 0)
            v_slots(first, lambda: None)
            period((0, 0), True)
            period((0, 1), True)
            with dve.Fori(1, PAIRS) as i:
                period((i, 0), True)
                period((i, 1), True)
            period((PAIRS, 0), True)
            period((PAIRS, 1), False)

        @block.gpsimd
        def _(pool):
            pool.memset(ident[:, :], 1.0).then_inc(s_id, 1)
            pool.wait_ge(s_id, 2)
            pool.affine_select(out=ident[:, :], in_=ident[:, :], compare_op=ALU.is_equal, fill=0.0, base=0,
                               pattern=[[-1, P]], channel_multiplier=1).then_inc(s_id, 1)

            def summed(b, t):
                hf, nt = divmod(t, NT)
                pool.wait_ge(s_p, cnt(b, G, t + 1))
                if nt == 1:
                    wait(pool, s_den, cnt(b, 2, hf - 1))
                if nt > 1:
                    pool.wait_ge(s_sum, cnt(b, G - 2, (NT - 1) * hf + nt - 1))
                acc_in = p32[:, (t - 1) % 4, :] if nt == 1 else psum_n[:, hf, :]
                pool.tensor_tensor(psum_n[:, hf, :], acc_in, p32[:, t % 4, :], ALU.add).then_inc(s_sum, 1)

            def finish(b, k):
                hf, ot = divmod(k, OT)
                pool.wait_ge(s_y[k % 2], cnt(b, U // 2, k // 2 + 1))
                pool.tensor_tensor(res[:, k, :], res[:, k, :], xs[:, b[1], ot, hf * HALF:(hf + 1) * HALF],
                                   ALU.add).then_inc(s_add, 1)

            def period(b, more):
                summed(b, NT + 2)
                summed(b, NT + 3)
                summed(b, NT + 4)
                summed(b, NT + 5)
                finish(b, 0)
                summed(b, NT + 6)
                summed(b, NT + 7)
                for k in range(1, 6):
                    finish(b, k)
                if more:
                    summed(nxt(b), 1)
                finish(b, 6)
                if more:
                    summed(nxt(b), 2)
                    summed(nxt(b), 3)
                finish(b, 7)
                if more:
                    for t in range(4, NT):
                        summed(nxt(b), t)
                    summed(nxt(b), NT + 1)

            for t in range(1, NT):
                summed(first, t)
            summed(first, NT + 1)
            period((0, 0), True)
            period((0, 1), True)
            with pool.Fori(1, PAIRS) as i:
                period((i, 0), True)
                period((i, 1), True)
            period((PAIRS, 0), True)
            period((PAIRS, 1), False)


_INS = ["x", "adj", "L0_gnn_wq", "L0_gnn_wk", "L0_gnn_bm"]


def kernel(**inputs):
    import numpy as _np
    import concourse.bacc as _bacc
    from concourse import mybir as _mybir
    from concourse.bass_utils import run_bass_kernel_spmd as _run

    nc = _bacc.Bacc("TRN2", target_bir_lowering=False, num_devices=1)
    arrays, args = {}, []
    for name in _INS:
        a = _np.ascontiguousarray(inputs[name])
        arrays[f"in_{name}_dram"] = a
        args.append(nc.dram_tensor(f"in_{name}_dram", a.shape, _mybir.dt.from_np(a.dtype), kind="ExternalInput").ap())
    shape = tuple(inputs["x"].shape)
    args.append(nc.dram_tensor("out_0_dram", shape, _mybir.dt.from_np(_np.dtype("float32")), kind="ExternalOutput").ap())
    gnn_layer(nc, *args)
    r = _run(nc, [arrays], core_ids=[0])
    return r.results[0]["out_0_dram"]
```

```python
from contextlib import ExitStack

import concourse.bass as bass
from concourse import mybir

F32 = mybir.dt.float32
F16 = mybir.dt.float16
I32 = mybir.dt.int32
ALU = mybir.AluOpType
ACT = mybir.ActivationFunctionType
AX = mybir.AxisListType

P = 128
H_SCALE = 2.0 ** 10
P_SCALE = 2.0 ** 15
SUM_SCALE = 2.0 ** 11
V_BITS = 2.0 ** 9
Q_BITS = 2.0 ** 12
EPS = 1e-5
LEAK = 0.01
NEWTON = 3


def gnn_layer(nc, x, adj, wq, wk, bm, out):
    B, C, N = x.shape
    O = adj.shape[0]
    CT, NT, OT = C // P, N // P, O // P
    HALF = N // 2
    MT = HALF // P
    U = 2 * OT
    G = 2 * NT
    assert C == O == 512 and HALF == 512 and B % 2 == 0
    PAIRS = B // 2 - 1

    with ExitStack() as ctx:
        def sb(name, shape, dt=F32):
            return ctx.enter_context(nc.sbuf_tensor(name, shape, dt))

        def bank(name):
            return ctx.enter_context(nc.psum_tensor(name, [P, 512], F32))

        def sem(name):
            return ctx.enter_context(nc.semaphore(name))

        xs = sb("xs", [P, 2, CT, N])
        h_hi = sb("h_hi", [P, 2, CT, N], F16)
        h_lo = sb("h_lo", [P, 2, CT, N], F16)
        h32 = sb("h32", [P, 2, N])
        v_hi = sb("v_hi", [P, NT, O], F16)
        v_lo = sb("v_lo", [P, NT, O], F16)
        p_hi = sb("p_hi", [P, 2, NT, HALF], F16)
        p_lo = sb("p_lo", [P, 2, NT, HALF], F16)
        p32 = sb("p32", [P, 4, HALF])
        leak32 = sb("leak32", [P, 4, HALF])
        psum_n = sb("psum_n", [P, 2, HALF])
        sum_hi = sb("sum_hi", [P, 2, HALF], F16)
        sum_lo = sb("sum_lo", [P, 2, HALF], F16)
        rden = sb("rden", [P, 2, HALF])
        normed = sb("normed", [P, 2, HALF])
        res = sb("res", [P, U, HALF])
        wmT_hi = sb("wmT_hi", [P, CT, O], F16)
        wmT_lo = sb("wmT_lo", [P, CT, O], F16)
        wqk = sb("wqk", [P, CT, 4], F16)
        ident = sb("ident", [P, P])
        ones = sb("ones", [P, 1], F16)
        bias_o = sb("bias_o", [P, OT])
        unscale_o = sb("unscale_o", [P, OT])
        unscale_q = sb("unscale_q", [P, 2])
        wm_nat = xs[:, 1, :, 0:C]
        wqk_row = res[:, 0:2, :]
        scrap = res[:, 2:8, :]
        wqk_col = sb("wqk_col", [P, 2, CT])
        rows = sb("rows", [P, OT + 2])
        pow2 = sb("pow2", [P, OT + 2])
        inv2 = sb("inv2", [P, OT + 2])
        stats = sb("stats", [P, CT, 2, 6])
        moments = sb("moments", [P, CT, 2])
        var_eps = sb("var_eps", [P, CT])
        rstd = sb("rstd", [P, CT])
        half_y2 = sb("half_y2", [P, CT])
        t_y = sb("t_y", [P, CT])
        ln_scale = sb("ln_scale", [P, 2, CT])
        ln_shift = sb("ln_shift", [P, 2, CT])
        qk4 = sb("qk4", [P, NT, 4])
        qk = sb("qk", [P, 2, NT])
        qs = sb("qs", [P, 2, NT])
        qmax_p = sb("qmax_p", [P, 1])
        qmax = sb("qmax", [P, 1])
        zcol = sb("zcol", [P, NT])
        log_A = sb("log_A", [P, NT])
        log_B = sb("log_B", [P, NT])
        A_col = sb("A_col", [P, NT])
        rcol = sb("rcol", [P, 2, MT])

        acc = [bank("acc0"), bank("acc1")]
        vps = [bank("vps0"), bank("vps1")]
        a_ps, b_ps, r_ps = bank("a_ps"), bank("b_ps"), bank("r_ps")
        small = bank("small")
        wmT_ps = vps + acc
        assert CT == 4
        qk_ps = small[:, 0:4 * NT].rearrange("p (t j) -> p t j", j=4)
        den_ps = small[:, 64:64 + 2 * MT].rearrange("p (h t) -> p h t", h=2)
        qmax_ps = small[:, 128:256]

        s_wv = sem("wq_wk_bm_loaded")
        s_w = sem("wm_loaded")
        s_wx = sem("x1_may_load")
        s_x = [[sem(f"x_loaded_{j}_{c}") for c in range(CT)] for j in range(2)]
        s_id = sem("constants_ready")
        s_abs = sem("abs_sums")
        s_su = sem("scaling_chain")
        s_wqk = sem("wqk_ready")
        s_wm = sem("wm_scaled")
        s_wt = sem("wmT_transposed")
        s_wh = sem("wmT_hi_ready")
        s_wl = sem("wmT_lo_ready")
        s_ln = sem("ln_chain")
        s_hhi = sem("h_hi_ready")
        s_h32 = sem("h32_ready")
        s_hlo = sem("h_split")
        s_qk = sem("qk_done")
        s_qc = sem("q_chain")
        s_qmT = sem("qmax_spread")
        s_exp = sem("exponentials")
        s_bc = sem("z_spread")
        s_cl = sem("log_ab_ready")
        s_a = sem("a_ready")
        s_lk = sem("leak_ready")
        s_p = sem("numerator_ready")
        s_phi = sem("p_hi_ready")
        s_plo = sem("p_lo_ready")
        s_sum = sem("numerator_summed")
        s_shi = sem("sum_hi_ready")
        s_slo = sem("sum_lo_ready")
        s_den = sem("denominator")
        s_rc = sem("reciprocal")
        s_rT = sem("reciprocal_spread")
        s_rd = sem("rden_ready")
        s_v = sem("v_psum_done")
        s_vhi = sem("v_hi_ready")
        s_vlo = [sem(f"v_split_{i}") for i in range(2)]
        s_acc = sem("unit_accumulated")
        s_nm = [sem(f"unit_normalised_{i}") for i in range(2)]
        s_y = [sem(f"relu_done_{i}") for i in range(2)]
        s_add = sem("unit_finished")
        s_st = [sem(f"stored_{k}") for k in range(U)]

        def nxt(b, by=1):
            j = b[1] + by
            return (b[0] + j // 2, j % 2)

        def cnt(b, per, n):
            return b[0] * (2 * per) + (b[1] * per + n)

        def wait(eng, semaphore, value):
            if not (isinstance(value, int) and value <= 0):
                eng.wait_ge(semaphore, value)

        first = (0, 0)

        LN_OPS = 3 + 3 * NEWTON + 2 + 1
        Q_OPS = 9

        block = ctx.enter_context(nc.Block())

        @block.sync
        def _(sp):
            def load_x(b, c):
                src = x[b[0] * 2 + b[1], c * P:(c + 1) * P, :]
                sp.dma_start(xs[:, b[1], c, :], src).then_inc(s_x[b[1]][c], 16)

            def store(b, k):
                hf, ot = divmod(k, OT)
                sp.wait_ge(s_add, cnt(b, U, k + 1))
                dst = out[b[0] * 2 + b[1], ot * P:(ot + 1) * P, hf * HALF:(hf + 1) * HALF]
                sp.dma_start(dst, res[:, k, :]).then_inc(s_st[k], 16)

            for c in range(CT):
                load_x(first, c)
            for i, w in enumerate((wq, wk)):
                sp.dma_start(wqk_row[:, i, :], w.partition_broadcast(P)).then_inc(s_wv, 16)
                with nc.allow_non_contiguous_dma(reason="512 weights, once"):
                    sp.dma_start(wqk_col[:, i, :], w.rearrange("(t p) -> p t", p=P)).then_inc(s_wv, 16)
            with nc.allow_non_contiguous_dma(reason="512 biases, once"):
                sp.dma_start(bias_o[:, :], bm.rearrange("(t p) -> p t", p=P)).then_inc(s_wv, 16)
            sp.dma_start(wm_nat, adj.rearrange("(t p) c -> p t c", p=P)).then_inc(s_w, 16)
            sp.wait_ge(s_wx, 1)
            for c in range(CT):
                load_x((0, 1), c)

            def period(b, load):
                for k in range(U):
                    store(b, k)
                    if load and k >= OT:
                        load_x(nxt(b, 2), k - OT)

            period((0, 0), True)
            period((0, 1), True)
            with sp.Fori(1, PAIRS) as i:
                period((i, 0), True)
                period((i, 1), True)
            period((PAIRS, 0), False)
            period((PAIRS, 1), False)
            for k in range(U):
                sp.wait_ge(s_st[k], 16 * B)

        @block.tensor
        def _(pe):
            def transposed_weights():
                pe.wait_ge(s_id, 3)
                pe.wait_ge(s_wm, 1)
                for ct in range(CT):
                    for ot in range(OT):
                        mm = pe.transpose(wmT_ps[ct][:, ot * P:(ot + 1) * P],
                                          wm_nat[:, ot, ct * P:(ct + 1) * P], ident[:, :])
                    mm.then_inc(s_wt, 1)

            def project_qk(b):
                pe.wait_ge(s_hlo, cnt(b, CT, CT))
                for nt in range(NT):
                    for ct in range(CT):
                        for part, hp in enumerate((h_hi, h_lo)):
                            mm = pe.matmul(qk_ps[:, nt, :], hp[:, b[1], ct, nt * P:(nt + 1) * P], wqk[:, ct, :],
                                           start=(ct == 0 and part == 0), stop=(ct == CT - 1 and part == 1))
                mm.then_inc(s_qk, 1)

            def spread_qmax(b):
                pe.wait_ge(s_qc, cnt(b, Q_OPS, 5))
                pe.transpose(qmax_ps, qmax_p[:, 0:1].to_broadcast([P, P]), ident[:, :]).then_inc(s_qmT, 1)

            def spread_z(b, hf):
                pe.wait_ge(s_qc, cnt(b, Q_OPS, 8))
                wait(pe, s_p, cnt(b, G, NT * hf))
                for t in range(MT):
                    mt = hf * MT + t
                    mm = pe.transpose(b_ps[:, t * P:(t + 1) * P],
                                      zcol[:, mt:mt + 1].to_broadcast([P, P]), ident[:, :])
                mm.then_inc(s_bc, 1)

            def v_tile(b, nt):
                wait(pe, s_vlo[nt % 2], cnt(b, NT // 2, nt // 2))
                ps, cols = vps[nt % 2], slice(nt * P, (nt + 1) * P)
                for ct in range(CT):
                    hi, lo = h_hi[:, b[1], ct, cols], h_lo[:, b[1], ct, cols]
                    pe.matmul(ps[:, :], hi, wmT_hi[:, ct, :], start=(ct == 0), stop=False)
                    pe.matmul(ps[:, :], hi, wmT_lo[:, ct, :], start=False, stop=False)
                    mm = pe.matmul(ps[:, :], lo, wmT_hi[:, ct, :], start=False, stop=(ct == CT - 1))
                mm.then_inc(s_v, 1)

            def unit(b, k, between=None):
                hf, ot = divmod(k, OT)
                wait(pe, s_nm[k % 2], cnt(b, U // 2, k // 2))
                ps, cols = acc[k % 2], slice(ot * P, (ot + 1) * P)
                for nt in range(NT):
                    if between and nt in between:
                        between[nt]()
                    if k == 0:
                        pe.wait_ge(s_vlo[nt % 2], cnt(b, NT // 2, nt // 2 + 1))
                    if ot == 0:
                        pe.wait_ge(s_plo, cnt(b, G, NT * hf + nt + 1))
                    pe.matmul(ps[:, :], v_hi[:, nt, cols], p_hi[:, hf, nt, :], start=(nt == 0), stop=False)
                    pe.matmul(ps[:, :], v_hi[:, nt, cols], p_lo[:, hf, nt, :], start=False, stop=False)
                    mm = pe.matmul(ps[:, :], v_lo[:, nt, cols], p_hi[:, hf, nt, :],
                                   start=False, stop=(nt == NT - 1))
                mm.then_inc(s_acc, 1)

            def denominator(b, hf):
                pe.wait_ge(s_slo, cnt(b, 2, hf + 1))
                for t in range(MT):
                    for part in (sum_hi, sum_lo):
                        mm = pe.matmul(den_ps[:, hf, t:t + 1], part[:, hf, t * P:(t + 1) * P], ones[:, :],
                                       start=(part is sum_hi), stop=(part is sum_lo))
                mm.then_inc(s_den, 1)

            def spread_reciprocal(b, hf):
                pe.wait_ge(s_rc, cnt(b, 2, hf + 1))
                for t in range(MT):
                    mm = pe.transpose(r_ps[:, t * P:(t + 1) * P],
                                      rcol[:, hf, t:t + 1].to_broadcast([P, P]), ident[:, :])
                mm.then_inc(s_rT, 1)

            def v_tiles(b, start=0):
                for nt in range(start, NT):
                    v_tile(b, nt)

            def period(b, more):
                unit(b, 0, {1: lambda: spread_z(b, 1), 3: lambda: denominator(b, 0)})
                spread_reciprocal(b, 0)
                for k in range(1, OT):
                    unit(b, k)
                unit(b, OT, {4: lambda: denominator(b, 1)})
                spread_reciprocal(b, 1)
                unit(b, OT + 1)
                unit(b, OT + 2)
                if more:
                    project_qk(nxt(b))
                unit(b, OT + 3, {4: lambda: spread_qmax(nxt(b))} if more else None)
                if more:
                    spread_z(nxt(b), 0)
                    v_tiles(nxt(b))

            transposed_weights()
            pe.wait_ge(s_wqk, 1)
            project_qk(first)
            spread_qmax(first)
            pe.wait_ge(s_wl, CT)
            v_tile(first, 0)
            spread_z(first, 0)
            v_tiles(first, 1)
            period((0, 0), True)
            period((0, 1), True)
            with pe.Fori(1, PAIRS) as i:
                period((i, 0), True)
                period((i, 1), True)
            period((PAIRS, 0), True)
            period((PAIRS, 1), False)

        @block.scalar
        def _(act):
            def absolute_sums():
                act.wait_ge(s_wv, 16 * 5)
                for i in range(2):
                    act.activation(scrap[:, OT + i, :], wqk_row[:, i, :], ACT.Abs,
                                   accum_out=rows[:, OT + i:OT + i + 1]).then_inc(s_abs, 1)
                act.wait_ge(s_w, 16)
                for ot in range(OT):
                    act.activation(scrap[:, ot, :], wm_nat[:, ot, :], ACT.Abs, accum_out=rows[:, ot:ot + 1]).then_inc(s_abs, 1)

            def weights_upper():
                for ct in range(CT):
                    act.wait_ge(s_wt, ct + 1)
                    act.activation(wmT_hi[:, ct, :], wmT_ps[ct][:, :], ACT.Copy).then_inc(s_wh, 1)

            def normalise(b, ct):
                if ct == 0:
                    act.wait_ge(s_ln, cnt(b, LN_OPS, LN_OPS))
                    wait(act, s_v, cnt(b, NT, -NT))
                act.activation(h_hi[:, b[1], ct, :], xs[:, b[1], ct, :], ACT.Relu, bias=ln_shift[:, b[1], ct:ct + 1],
                               scale=ln_scale[:, b[1], ct:ct + 1]).then_inc(s_hhi, 1)

            def exponentials(b):
                act.wait_ge(s_qc, cnt(b, Q_OPS, 8))
                act.activation(A_col[:, :], log_A[:, :], ACT.Exp).then_inc(s_exp, 1)

            def a_of(b, hf):
                act.wait_ge(s_cl, cnt(b, 4, 2 * hf + 1))
                act.activation(a_ps[:, :], a_ps[:, :], ACT.Exp).then_inc(s_a, 1)

            def leak(b, t):
                hf, nt = divmod(t, NT)
                if nt == 0:
                    act.wait_ge(s_cl, cnt(b, 4, 2 * hf + 2))
                    act.wait_ge(s_qc, cnt(b, Q_OPS, 9))
                wait(act, s_p, cnt(b, G, t - 3))
                act.activation(leak32[:, t % 4, :], b_ps[:, :], ACT.Exp,
                               bias=log_B[:, nt:nt + 1]).then_inc(s_lk, 1)

            def p_upper(b, t):
                hf, nt = divmod(t, NT)
                act.wait_ge(s_p, cnt(b, G, t + 1))
                if nt == 0:
                    wait(act, s_acc, cnt(b, U, OT * (hf + 1) - U))
                act.activation(p_hi[:, hf, nt, :], p32[:, t % 4, :], ACT.Copy, scale=P_SCALE).then_inc(s_phi, 1)

            def v_upper(b, nt):
                act.wait_ge(s_v, cnt(b, NT, nt + 1))
                act.activation(v_hi[:, nt, :], vps[nt % 2][:, :], ACT.Copy,
                               scale=1.0 / H_SCALE).then_inc(s_vhi, 1)

            def relu(b, k):
                hf, ot = divmod(k, OT)
                act.wait_ge(s_nm[k % 2], cnt(b, U // 2, k // 2 + 1))
                wait(act, s_st[k], cnt(b, 16, 0))
                act.activation(res[:, k, :], normed[:, k % 2, :], ACT.Relu, bias=bias_o[:, ot:ot + 1],
                               scale=unscale_o[:, ot:ot + 1]).then_inc(s_y[k % 2], 1)

            def copy_reciprocal(b, hf):
                act.wait_ge(s_rT, cnt(b, 2, hf + 1))
                act.activation(rden[:, hf, :], r_ps[:, :], ACT.Copy).then_inc(s_rd, 1)

            def sum_upper(b, hf):
                act.wait_ge(s_sum, cnt(b, G - 2, (NT - 1) * (hf + 1)))
                act.activation(sum_hi[:, hf, :], psum_n[:, hf, :], ACT.Copy, scale=SUM_SCALE).then_inc(s_shi, 1)

            def leaks(b, t):
                leak(b, t)
                leak(b, t + 1)

            def p_uppers(b, t):
                p_upper(b, t)
                p_upper(b, t + 1)

            def v_slots(b, before):
                a_of(b, 0)
                leaks(b, 0)
                before()
                for m in range(NT // 2):
                    v_upper(b, 2 * m)
                    p_uppers(b, 2 * m)
                    if m < NT // 2 - 1:
                        leaks(b, 2 * m + 2)
                    else:
                        sum_upper(b, 0)
                    v_upper(b, 2 * m + 1)

            def period(b, more):
                a_of(b, 1)
                leaks(b, NT)
                p_uppers(b, NT)
                leaks(b, NT + 2)
                copy_reciprocal(b, 0)
                relu(b, 0)
                p_uppers(b, NT + 2)
                leaks(b, NT + 4)
                relu(b, 1)
                p_uppers(b, NT + 4)
                leaks(b, NT + 6)
                relu(b, 2)
                p_uppers(b, NT + 6)
                sum_upper(b, 1)
                relu(b, 3)
                if more:
                    normalise(nxt(b), 0)
                    normalise(nxt(b), 1)
                copy_reciprocal(b, 1)
                if more:
                    normalise(nxt(b), 2)
                    normalise(nxt(b), 3)
                relu(b, 4)
                relu(b, 5)
                relu(b, 6)
                if more:
                    exponentials(nxt(b))
                    v_slots(nxt(b), lambda: relu(b, 7))
                else:
                    relu(b, 7)

            absolute_sums()
            for ct in range(CT):
                normalise(first, ct)
            weights_upper()
            exponentials(first)
            v_slots(first, lambda: None)
            period((0, 0), True)
            period((0, 1), True)
            with act.Fori(1, PAIRS) as i:
                period((i, 0), True)
                period((i, 1), True)
            period((PAIRS, 0), True)
            period((PAIRS, 1), False)

        @block.vector
        def _(dve):
            def scaled_weights():
                n = [0]

                def link(ins):
                    n[0] += 1
                    ins.then_inc(s_su, 1)
                    dve.wait_ge(s_su, n[0])

                dve.wait_ge(s_abs, OT + 2)
                link(dve.tensor_scalar(rows[:, :], rows[:, :], 1e-25, 1e30, ALU.max, ALU.min))
                link(dve.tensor_scalar(pow2[:, :].bitcast(I32), rows[:, :].bitcast(I32), 0x7F800000, None,
                                       ALU.bitwise_and))
                link(dve.reciprocal(inv2[:, :], pow2[:, :]))
                for i in range(2):
                    dve.tensor_scalar(wqk_col[:, i, :], wqk_col[:, i, :], inv2[:, OT + i:OT + i + 1], Q_BITS,
                                      ALU.mult, ALU.mult).then_inc(s_su, 1)
                dve.tensor_scalar(unscale_o[:, :], pow2[:, 0:OT], SUM_SCALE / P_SCALE / V_BITS, None, ALU.mult).then_inc(s_su, 1)
                dve.tensor_scalar(unscale_q[:, :], pow2[:, OT:OT + 2], 1.0 / (Q_BITS * H_SCALE), None,
                                  ALU.mult).then_inc(s_su, 1)
                n[0] += 4
                dve.wait_ge(s_su, n[0])
                hi = wqk[:, :, :].rearrange("p t (i s) -> p s i t", s=2)
                link(dve.tensor_copy(hi[:, 0], wqk_col[:, :, :]))
                dve.tensor_tensor(hi[:, 1], wqk_col[:, :, :], hi[:, 0], ALU.subtract).then_inc(s_wqk, 1)

            def weights_lower():
                for ct in range(CT):
                    dve.wait_ge(s_wh, ct + 1)
                    dve.tensor_tensor(wmT_lo[:, ct, :], wmT_ps[ct][:, :], wmT_hi[:, ct, :],
                                      ALU.subtract).then_inc(s_wl, 1)
                dve.wait_ge(s_wt, CT)
                dve.memset(t_y[:, 0:1], 0.0).then_inc(s_wx, 1)

            def statistics(b, cts):
                for ct in cts:
                    dve.wait_ge(s_x[b[1]][ct], (b[0] + 1) * 16)
                    for s in range(2):
                        ins = dve.bn_stats(stats[:, ct, s, :], xs[:, b[1], ct, s * HALF:(s + 1) * HALF])
                if cts[-1] == CT - 1:
                    ins.then_inc(s_ln, 1)

            def normaliser(b):
                n = [1]

                def link(ins):
                    ins.then_inc(s_ln, 1)
                    n[0] += 1
                    dve.wait_ge(s_ln, cnt(b, LN_OPS, n[0]))

                dve.wait_ge(s_ln, cnt(b, LN_OPS, 1))
                dve.memset(half_y2[:, :], 0.0)
                for ct in range(CT):
                    ins = dve.bn_aggr(moments[:, ct, :], stats[:, ct, :, :].rearrange("p s j -> p (s j)"))
                link(ins)
                link(dve.tensor_scalar(var_eps[:, :], moments[:, :, 1], EPS, None, ALU.add))
                link(dve.tensor_scalar(rstd[:, :].bitcast(I32), var_eps[:, :].bitcast(I32), -0.5, float(0x5F3759DF),
                                       ALU.mult, ALU.add))
                for _ in range(NEWTON):
                    link(dve.scalar_tensor_tensor(out=half_y2[:, :], in0=rstd[:, :], scalar=-0.5, in1=rstd[:, :],
                                                  op0=ALU.mult, op1=ALU.mult))
                    link(dve.tensor_tensor(t_y[:, :], half_y2[:, :], var_eps[:, :], ALU.mult))
                    link(dve.scalar_tensor_tensor(out=rstd[:, :], in0=t_y[:, :], scalar=1.5, in1=rstd[:, :],
                                                  op0=ALU.add, op1=ALU.mult))
                link(dve.tensor_scalar(ln_scale[:, b[1], :], rstd[:, :], H_SCALE, None, ALU.mult))
                dve.scalar_tensor_tensor(out=ln_shift[:, b[1], :], in0=moments[:, :, 0], scalar=-H_SCALE,
                                         in1=rstd[:, :], op0=ALU.mult, op1=ALU.mult).then_inc(s_ln, 1)
                assert n[0] + 1 == LN_OPS
                dve.wait_ge(s_ln, cnt(b, LN_OPS, LN_OPS))

            def h_full(b, cts):
                for ct in cts:
                    wait(dve, s_hlo, cnt(b, CT, ct - 1))
                    dve.tensor_scalar(h32[:, ct % 2, :], xs[:, b[1], ct, :], ln_scale[:, b[1], ct:ct + 1],
                                      ln_shift[:, b[1], ct:ct + 1], ALU.mult, ALU.add).then_inc(s_h32, 1)

            def h_rest(b, cts):
                for ct in cts:
                    dve.wait_ge(s_hhi, cnt(b, CT, ct + 1))
                    dve.wait_ge(s_h32, cnt(b, CT, ct + 1))
                    dve.scalar_tensor_tensor(out=h_lo[:, b[1], ct, :], in0=h32[:, ct % 2, :], scalar=0.0,
                                             in1=h_hi[:, b[1], ct, :], op0=ALU.max,
                                             op1=ALU.subtract).then_inc(s_hlo, 1)

            def h_lower(b, cts):
                h_full(b, cts)
                h_rest(b, cts)

            def q_link(b, n, ins):
                ins.then_inc(s_qc, 1)
                dve.wait_ge(s_qc, cnt(b, Q_OPS, n))

            def q_head(b):
                dve.wait_ge(s_qk, cnt(b, 1, 1))
                q_link(b, 1, dve.tensor_copy(qk4[:, :, :], qk_ps))
                parts = qk4[:, :, :].rearrange("p t (i s) -> p s i t", s=2)
                q_link(b, 2, dve.tensor_tensor(qs[:, :, :], parts[:, 0], parts[:, 1], ALU.add))
                for i in range(2):
                    q_link(b, 3 + i, dve.tensor_scalar(qk[:, i, :], qs[:, i, :], unscale_q[:, i:i + 1], None,
                                                       ALU.mult))
                dve.tensor_reduce(qmax_p[:, :], qk[:, 0, :], AX.X, ALU.max).then_inc(s_qc, 1)

            def q_tail(b):
                dve.wait_ge(s_qmT, cnt(b, 1, 1))
                q_link(b, 6, dve.tensor_reduce(qmax[:, :], qmax_ps, AX.X, ALU.max))
                dve.tensor_scalar(log_A[:, :], qk[:, 0, :], qmax[:, 0:1], None, ALU.subtract).then_inc(s_qc, 1)
                dve.tensor_scalar(zcol[:, :], qk[:, 1, :], qmax[:, 0:1], None, ALU.add).then_inc(s_qc, 1)
                dve.wait_ge(s_qc, cnt(b, Q_OPS, 8))
                dve.tensor_scalar(log_B[:, :], log_A[:, :], LEAK, None, ALU.mult).then_inc(s_qc, 1)

            def log_ab(b, hf):
                dve.wait_ge(s_bc, cnt(b, 2, hf + 1))
                for c, (dst, slope) in enumerate(((a_ps, 1.0 - LEAK), (b_ps, LEAK - 1.0))):
                    if c == 1:
                        dve.wait_ge(s_cl, cnt(b, 4, 2 * hf + 1))
                    dve.tensor_scalar(dst[:, :], b_ps[:, :], slope, 0.0, ALU.mult, ALU.min).then_inc(s_cl, 1)

            def numerator(b, t):
                hf, nt = divmod(t, NT)
                if nt == 0:
                    dve.wait_ge(s_exp, cnt(b, 1, 1))
                    dve.wait_ge(s_a, cnt(b, 2, hf + 1))
                dve.wait_ge(s_lk, cnt(b, G, t + 1))
                ago = t - 4
                wait(dve, s_sum, cnt(b, G - 2, (NT - 1) * (ago // NT) + max(ago % NT, 1)))
                dve.scalar_tensor_tensor(out=p32[:, t % 4, :], in0=a_ps[:, :], scalar=A_col[:, nt:nt + 1],
                                         in1=leak32[:, t % 4, :], op0=ALU.mult, op1=ALU.max).then_inc(s_p, 1)

            def p_lower(b, t):
                hf, nt = divmod(t, NT)
                dve.wait_ge(s_phi, cnt(b, G, t + 1))
                dve.scalar_tensor_tensor(out=p_lo[:, hf, nt, :], in0=p32[:, t % 4, :], scalar=P_SCALE,
                                         in1=p_hi[:, hf, nt, :], op0=ALU.mult, op1=ALU.subtract).then_inc(s_plo, 1)

            def numerators(b, t):
                numerator(b, t)
                numerator(b, t + 1)

            def p_lowers(b, t):
                p_lower(b, t)
                p_lower(b, t + 1)

            def sum_lower(b, hf):
                dve.wait_ge(s_shi, cnt(b, 2, hf + 1))
                dve.scalar_tensor_tensor(out=sum_lo[:, hf, :], in0=psum_n[:, hf, :], scalar=SUM_SCALE,
                                         in1=sum_hi[:, hf, :], op0=ALU.mult, op1=ALU.subtract).then_inc(s_slo, 1)

            def v_lower(b, nt):
                dve.wait_ge(s_vhi, cnt(b, NT, nt + 1))
                dve.scalar_tensor_tensor(out=v_lo[:, nt, :], in0=vps[nt % 2][:, :], scalar=1.0 / H_SCALE,
                                         in1=v_hi[:, nt, :], op0=ALU.mult,
                                         op1=ALU.subtract).then_inc(s_vlo[nt % 2], 1)

            def reciprocal(b, hf):
                dve.wait_ge(s_den, cnt(b, 2, hf + 1))
                dve.reciprocal(rcol[:, hf, :], den_ps[:, hf, :]).then_inc(s_rc, 1)

            def normalised(b, k):
                hf, ot = divmod(k, OT)
                if ot == 0:
                    dve.wait_ge(s_rd, cnt(b, 2, hf + 1))
                dve.wait_ge(s_acc, cnt(b, U, k + 1))
                wait(dve, s_y[k % 2], cnt(b, U // 2, k // 2))
                dve.tensor_tensor(normed[:, k % 2, :], acc[k % 2][:, :], rden[:, hf, :],
                                  ALU.mult).then_inc(s_nm[k % 2], 1)

            def v_slots(b, before):
                log_ab(b, 0)
                before()
                for m in range(NT // 2):
                    numerators(b, 2 * m)
                    v_lower(b, 2 * m)
                    p_lowers(b, 2 * m)
                    if m == NT // 2 - 1:
                        sum_lower(b, 0)
                    v_lower(b, 2 * m + 1)

            def period(b, more):
                log_ab(b, 1)
                for m in range(NT // 2):
                    if m > 0:
                        normalised(b, m - 1)
                    numerators(b, NT + 2 * m)
                    if m == 0:
                        reciprocal(b, 0)
                    if more:
                        statistics(nxt(b), [m])
                    p_lowers(b, NT + 2 * m)
                sum_lower(b, 1)
                if more:
                    normaliser(nxt(b))
                normalised(b, 3)
                reciprocal(b, 1)
                if more:
                    h_lower(nxt(b), [0, 1])
                normalised(b, 4)
                if more:
                    h_lower(nxt(b), [2, 3])
                normalised(b, 5)
                if more:
                    q_head(nxt(b))
                normalised(b, 6)
                if more:
                    q_tail(nxt(b))
                    v_slots(nxt(b), lambda: normalised(b, 7))
                else:
                    normalised(b, 7)

            dve.memset(ones[:, :], 1.0).then_inc(s_id, 1)
            statistics(first, [0, 1, 2, 3])
            normaliser(first)
            h_full(first, [0, 1])
            scaled_weights()
            h_rest(first, [0, 1])
            h_lower(first, [2, 3])
            weights_lower()
            q_head(first)
            q_tail(first)
            v_slots(first, lambda: None)
            period((0, 0), True)
            period((0, 1), True)
            with dve.Fori(1, PAIRS) as i:
                period((i, 0), True)
                period((i, 1), True)
            period((PAIRS, 0), True)
            period((PAIRS, 1), False)

        @block.gpsimd
        def _(pool):
            pool.memset(ident[:, :], 1.0).then_inc(s_id, 1)
            pool.wait_ge(s_id, 2)
            pool.affine_select(out=ident[:, :], in_=ident[:, :], compare_op=ALU.is_equal, fill=0.0, base=0,
                               pattern=[[-1, P]], channel_multiplier=1).then_inc(s_id, 1)
            pool.wait_ge(s_su, 3)
            for ot in range(OT):
                ins = pool.tensor_scalar(wm_nat[:, ot, :], wm_nat[:, ot, :], inv2[:, ot:ot + 1], V_BITS,
                                         ALU.mult, ALU.mult)
            ins.then_inc(s_wm, 1)

            def summed(b, t):
                hf, nt = divmod(t, NT)
                pool.wait_ge(s_p, cnt(b, G, t + 1))
                if nt == 1:
                    wait(pool, s_den, cnt(b, 2, hf - 1))
                if nt > 1:
                    pool.wait_ge(s_sum, cnt(b, G - 2, (NT - 1) * hf + nt - 1))
                acc_in = p32[:, (t - 1) % 4, :] if nt == 1 else psum_n[:, hf, :]
                pool.tensor_tensor(psum_n[:, hf, :], acc_in, p32[:, t % 4, :], ALU.add).then_inc(s_sum, 1)

            def finish(b, k):
                hf, ot = divmod(k, OT)
                pool.wait_ge(s_y[k % 2], cnt(b, U // 2, k // 2 + 1))
                pool.tensor_tensor(res[:, k, :], res[:, k, :], xs[:, b[1], ot, hf * HALF:(hf + 1) * HALF],
                                   ALU.add).then_inc(s_add, 1)

            def period(b, more):
                summed(b, NT + 1)
                for m in range(1, NT // 2):
                    summed(b, NT + 2 * m)
                    summed(b, NT + 2 * m + 1)
                    finish(b, m - 1)
                for k in range(NT // 2 - 1, U):
                    finish(b, k)
                if more:
                    for t in range(1, NT):
                        summed(nxt(b), t)

            for t in range(1, NT):
                summed(first, t)
            period((0, 0), True)
            period((0, 1), True)
            with pool.Fori(1, PAIRS) as i:
                period((i, 0), True)
                period((i, 1), True)
            period((PAIRS, 0), True)
            period((PAIRS, 1), False)


_INS = ["x", "adj", "L0_gnn_wq", "L0_gnn_wk", "L0_gnn_bm"]


def kernel(**inputs):
    import numpy as _np
    import concourse.bacc as _bacc
    from concourse import mybir as _mybir
    from concourse.bass_utils import run_bass_kernel_spmd as _run

    nc = _bacc.Bacc("TRN2", target_bir_lowering=False, num_devices=1)
    arrays, args = {}, []
    for name in _INS:
        a = _np.ascontiguousarray(inputs[name])
        arrays[f"in_{name}_dram"] = a
        args.append(nc.dram_tensor(f"in_{name}_dram", a.shape, _mybir.dt.from_np(a.dtype), kind="ExternalInput").ap())
    shape = tuple(inputs["x"].shape)
    args.append(nc.dram_tensor("out_0_dram", shape, _mybir.dt.from_np(_np.dtype("float32")), kind="ExternalOutput").ap())
    gnn_layer(nc, *args)
    r = _run(nc, [arrays], core_ids=[0])
    return r.results[0]["out_0_dram"]
```
